# Optimizing a Trainium2 kernel written in Bass

```python
import numpy as np
import jax
import jax.numpy as jnp

def _softmax(x, axis=-1):
    return jax.nn.softmax(x, axis=axis)

def _gelu(x):
    return jax.nn.gelu(x, approximate=True)

def _silu(x):
    return jax.nn.silu(x)

def _sigmoid(x):
    return jax.nn.sigmoid(x)

def _layernorm(x, axis=-1, eps=1e-05):
    m = jnp.mean(x, axis=axis, keepdims=True)
    v = jnp.var(x, axis=axis, keepdims=True)
    return (x - m) / jnp.sqrt(v + eps)

def _scatter_add(tgt, idx, src, axis=0):
    return tgt.at[idx].add(src)

def _segment_sum(src, seg, n):
    return jax.ops.segment_sum(src, seg, n)
kernel_name = 'mk_adj_resnorm_d1_adj_r2_415a81'

def setup_inputs(seed: int=0):
    np.random.seed(seed)
    _w = jnp.asarray

    def _rec_inputs():
        import jax
        import jax.numpy as jnp
        _gk = jax.random.key(seed)
        x = 0.0002279 + 0.9999 * jax.random.normal(jax.random.fold_in(_gk, 1), (4096, 128), jnp.float32)
        _a = jax.random.bernoulli(jax.random.fold_in(_gk, 2), 0.00195312, (4096, 4096))
        _a = jnp.logical_or(_a, jnp.swapaxes(_a, -1, -2))
        _a = jnp.logical_or(_a, jnp.eye(4096, dtype=bool))
        adj = _a.astype(jnp.int32)
        return (x, adj)
    x, adj = _rec_inputs()

    def _L0_gnn_setup():
        import jax, jax.numpy as jnp
        import numpy as np
        N, D = (4096, 128)
        key = jax.random.key(seed)
        k1, k2, k3 = jax.random.split(key, 3)
        adj = jax.random.randint(k1, (N, N), 0, 2, dtype=jnp.int32)
        emb = jax.random.normal(k2, (N, D), dtype=jnp.float32)
        attn = jax.random.normal(k3, (2 * D, 1), dtype=jnp.float32)
        return {'adj': adj, 'emb': emb, 'attn': attn}
    _L0_gnn_all = _L0_gnn_setup()
    _L0_gnn_in = {k: v for k, v in _L0_gnn_all.items() if k in ('attn',)}
    del _L0_gnn_all
    return {'x': x, 'adj': adj, 'L0_gnn_attn': _L0_gnn_in['attn']}

def reference(x, adj, L0_gnn_attn):
    import jax
    import jax.numpy as jnp

    def _L0_gnn_ref(adj, emb, attn):
        import jax, jax.numpy as jnp
        import numpy as np
        N, D = (4096, 128)
        d = emb.shape[1]
        s_i = emb @ attn[:d]
        s_j = emb @ attn[d:]
        e = jax.nn.leaky_relu(s_i + s_j.T, negative_slope=0.2)
        neg_inf = jnp.float32(-1000000000.0)
        e = e + jnp.where(adj > 0, jnp.float32(0.0), neg_inf)
        alpha = jax.nn.softmax(e, axis=1)
        return alpha @ emb
    x = _layernorm(x + _L0_gnn_ref(adj, x, L0_gnn_attn), axis=-1)
    return x

_drawn_inputs = setup_inputs


def setup_inputs(seed=0):
    import zlib

    import numpy as np

    out = dict(_drawn_inputs(seed))
    spreads = {}
    factors = {}
    for name, (base, spread) in spreads.items():
        noise = np.random.default_rng([zlib.crc32(name.encode()), seed]).standard_normal(out[name].shape)
        drawn = base * np.exp(spread * noise) if base else spread * noise
        out[name] = jnp.asarray(drawn.astype(out[name].dtype))
    for name, factor in factors.items():
        out[name] = (out[name] * factor).astype(out[name].dtype)
    return out
```

```python
import concourse.bass as bass
from concourse import mybir
from contextlib import ExitStack



def gat_kernel(nc: bass.Bass, x: bass.AP, adj: bass.AP, attn: bass.AP, out: bass.AP):
    fp32 = mybir.dt.float32
    i32 = mybir.dt.int32
    u8 = mybir.dt.uint8
    u32 = mybir.dt.uint32
    ALU = mybir.AluOpType
    ACT = mybir.ActivationFunctionType
    X = mybir.AxisListType.X

    P = 128
    N, D = x.shape
    TILES = N // P
    Q = 4
    QC = N // Q
    B = 32
    K = 4
    FB = QC // (B * K)
    CHUNKS = FB * K
    D1 = D + 1
    PITCH = D + 2
    BLOCKS = [1, 1, 2, 4, 8, 8, 8]
    FIRST = [sum(BLOCKS[:s]) for s in range(len(BLOCKS))]
    MAXT = max(BLOCKS)
    NB = len(BLOCKS)
    ADJ_SLOTS = 4
    BYTE_SLOTS = 2
    W_SLOTS = K
    SLOPE = 0.2
    EPS = 1e-5
    BANK = 512
    RB = N // BANK

    adj_v = adj.rearrange("(t g a) (q c) -> t q a g c", g=P // B, a=B, q=Q)
    xj_v = x.rearrange("(pb fb b k) d -> pb b fb k d", pb=Q, fb=FB, b=B)
    xi_v = x.rearrange("(t p) d -> p t d", p=P)
    out_v = out.rearrange("(t p) d -> p t d", p=P)

    with ExitStack() as ctx:
        def sb(name, shape, dt):
            return ctx.enter_context(nc.sbuf_tensor(name, shape, dt))

        def sem(name):
            return ctx.enter_context(nc.semaphore(name))

        adj_in = sb("adj_in", [P, ADJ_SLOTS, P // B, QC], i32)
        mask_bytes = sb("mask_bytes", [P, BYTE_SLOTS, P // B, QC], u8)
        mask_t = sb("mask_t", [P, 2, FB, MAXT * P, K], u8)
        weights = sb("weights", [P, W_SLOTS, MAXT * P], fp32)
        xj = sb("xj", [P, CHUNKS, PITCH], fp32)
        q_row = sb("q_row", [P, N], fp32)
        agg = sb("agg", [P, MAXT, PITCH], fp32)
        y = sb("y", [P, MAXT, D], fp32)
        attn_i = sb("attn_i", [P, 1], fp32)
        attn_iw = sb("attn_iw", [P, P], fp32)
        attn_j = sb("attn_j", [P, D], fp32)
        ident = sb("ident", [P, P], fp32)
        ones = sb("ones", [P, P], fp32)
        s_j = sb("s_j", [P, CHUNKS], fp32)
        r_j = sb("r_j", [P, CHUNKS], fp32)
        d_j = sb("d_j", [P, CHUNKS], fp32)
        smax = sb("smax", [P, 2], fp32)
        shift = sb("shift", [P, 2], fp32)
        rden = sb("rden", [P, MAXT], fp32)
        total = sb("total", [P, MAXT], fp32)
        neg_mean = sb("neg_mean", [P, MAXT], fp32)
        square_sum = sb("square_sum", [P, MAXT], fp32)
        variance = sb("variance", [P, MAXT], fp32)
        half = sb("half", [P, MAXT], fp32)
        rstd = sb("rstd", [P, MAXT], fp32)
        offset = sb("offset", [P, MAXT], fp32)
        sig_bias = sb("sig_bias", [P, 1], fp32)

        spare = mask_t[:, 1, :, :, :].rearrange("p f i k -> p (f i k)").bitcast(fp32)
        xT = spare[:, 0:N]
        prod = spare[:, N:2 * N]

        banks = [ctx.enter_context(nc.psum_tensor(f"bank{i}", [P, BANK], fp32)) for i in range(8)]

        x_loaded = sem("x_loaded")
        attn_loaded = sem("attn_loaded")
        xi_loaded = sem("xi_loaded")
        adj_loaded = [sem(f"adj_loaded{i}") for i in range(ADJ_SLOTS)]
        out_stored = sem("out_stored")
        ident_zeroed = sem("ident_zeroed")
        consts_ready = sem("consts_ready")
        attn_wide = sem("attn_wide")
        xT_in_psum = sem("xT_in_psum")
        xT_ready = sem("xT_ready")
        s_i_in_psum = sem("s_i_in_psum")
        products_ready = sem("products_ready")
        s_j_ready = sem("s_j_ready")
        row_max_ready = sem("row_max_ready")
        max_turned = sem("max_turned")
        max_found = sem("max_found")
        max_spread = sem("max_spread")
        shift_ready = sem("shift_ready")
        factors_ready = sem("factors_ready")
        q_exp_ready = sem("q_exp_ready")
        q_ready = sem("q_ready")
        xj_scaled = sem("xj_scaled")
        bytes_ready = sem("bytes_ready")
        mask_ready = sem("mask_ready")
        weights_ready = sem("weights_ready")
        weights_used = sem("weights_used")
        tile_summed = sem("tile_summed")
        tile_copied = sem("tile_copied")
        rden_ready = sem("rden_ready")
        y_ready = sem("y_ready")
        total_ready = sem("total_ready")
        mean_ready = sem("mean_ready")
        squares_ready = sem("squares_ready")
        variance_ready = sem("variance_ready")
        rstd_ready = sem("rstd_ready")
        offset_ready = sem("offset_ready")
        out_ready = sem("out_ready")

        block = ctx.enter_context(nc.Block())

        @block.sync
        def _(sp):
            for pb in range(Q):
                for fb in range(FB):
                    sp.dma_start(xj[B * pb:B * (pb + 1), fb * K:(fb + 1) * K, 0:D],
                                 xj_v[pb, :, fb, :, :]).then_inc(x_loaded, 16)
            sp.dma_start(attn_i[:], attn[0:D, :]).then_inc(attn_loaded, 16)
            sp.dma_start(attn_j[:], attn[D:2 * D, :].rearrange("d o -> o d").broadcast_to([P, D])).then_inc(attn_loaded, 16)

            def load_tile(t, slot):
                for q in range(Q):
                    sp.dma_start(adj_in[B * q:B * (q + 1), slot, :, :],
                                 adj_v[bass.ds(t, 1), q, :, :, :].rearrange("o a g c -> (o a) g c")
                                 ).then_inc(adj_loaded[slot], 16)

            for t in range(ADJ_SLOTS):
                load_tile(t, t)
            with sp.Fori(1, TILES // ADJ_SLOTS) as turn:
                for slot in range(ADJ_SLOTS):
                    sp.wait_ge(bytes_ready, (turn - 1) * ADJ_SLOTS + (slot + 1))
                    load_tile(turn * ADJ_SLOTS + slot, slot)

        @block.gpsimd
        def _(pool):
            nc.gpsimd.memset(ident[:], 0.0).then_inc(ident_zeroed, 1)
            nc.gpsimd.memset(ones[:], 1.0)
            nc.gpsimd.memset(half[:], -0.5)
            nc.gpsimd.memset(sig_bias[:], -100.0)
            pool.wait_ge(ident_zeroed, 1)
            nc.gpsimd.affine_select(out=ident[:], in_=ident[:], compare_op=ALU.not_equal, fill=1.0, base=0,
                                    pattern=[[-1, P]], channel_multiplier=1).then_inc(consts_ready, 1)
            nc.gpsimd.dma_start(y[:, 0:BLOCKS[0], :], xi_v[:, 0:BLOCKS[0], :]).then_inc(xi_loaded, 16)
            for s in range(NB):
                n = BLOCKS[s]
                pool.wait_ge(total_ready, s + 1)
                nc.gpsimd.tensor_scalar(neg_mean[:, 0:n], total[:, 0:n], -1.0 / D, 0.0,
                                        ALU.mult, ALU.add).then_inc(mean_ready, 1)
                pool.wait_ge(squares_ready, s + 1)
                nc.gpsimd.tensor_scalar(variance[:, 0:n], square_sum[:, 0:n], 1.0 / D, EPS,
                                        ALU.mult, ALU.add).then_inc(variance_ready, 1)
                pool.wait_ge(variance_ready, s + 1)
                nc.gpsimd.tensor_tensor(rstd[:, 0:n], variance[:, 0:n], half[:, 0:n], ALU.pow).then_inc(rstd_ready, 1)
                pool.wait_ge(rstd_ready, s + 1)
                nc.gpsimd.tensor_tensor(offset[:, 0:n], neg_mean[:, 0:n], rstd[:, 0:n],
                                        ALU.mult).then_inc(offset_ready, 1)
                if s + 1 < NB:
                    pool.wait_ge(out_stored, 16 * (s + 1))
                    nc.gpsimd.dma_start(y[:, 0:BLOCKS[s + 1], :],
                                        xi_v[:, FIRST[s + 1]:FIRST[s + 1] + BLOCKS[s + 1], :]).then_inc(xi_loaded, 16)

        @block.scalar
        def _(act):
            xT_v = xT.rearrange("d (pb fb b k) -> d fb k pb b", pb=Q, fb=FB, b=B)
            for fb in range(FB):
                act.wait_ge(xT_in_psum, fb + 1)
                for k in range(K):
                    last = nc.scalar.copy(xT_v[:, fb, k, :, :],
                                   banks[fb % 4][:, k * P:(k + 1) * P].rearrange("d (pb b) -> d pb b", pb=Q))
                last.then_inc(xT_ready, 1)
            act.wait_ge(shift_ready, 1)
            nc.scalar.activation(r_j[:], s_j[:], ACT.Exp, bias=shift[:, 0:1], scale=1 - SLOPE)
            nc.scalar.activation(d_j[:], s_j[:], ACT.Exp, bias=shift[:, 1:2], scale=SLOPE).then_inc(factors_ready, 1)
            nc.scalar.activation(xj[:, :, D], s_j[:], ACT.Exp, bias=shift[:, 1:2], scale=SLOPE)
            for rb in range(RB):
                act.wait_ge(s_i_in_psum, rb + 1)
                nc.scalar.activation(q_row[:, rb * BANK:(rb + 1) * BANK], banks[rb % (RB - 1)][:, :], ACT.Exp,
                                     bias=shift[:, 0:1], scale=SLOPE - 1).then_inc(q_exp_ready, 1)

            def to_bytes(t):
                act.wait_ge(adj_loaded[t % ADJ_SLOTS], 16 * Q * (t // ADJ_SLOTS + 1))
                if t >= BYTE_SLOTS:
                    act.wait_ge(mask_ready, t - BYTE_SLOTS + 1)
                nc.scalar.activation(mask_bytes[:, t % BYTE_SLOTS, :, :], adj_in[:, t % ADJ_SLOTS, :, :],
                                     ACT.Sigmoid, bias=sig_bias[:], scale=200.0).then_inc(bytes_ready, 1)

            def copy_sums(s):
                n, t0 = BLOCKS[s], FIRST[s]
                if s >= 1:
                    act.wait_ge(y_ready, s)
                for t in range(n):
                    if t < n - 1:
                        act.wait_ge(tile_summed, t0 - s + t + 1)
                    else:
                        act.wait_ge(weights_used, (s + 1) * CHUNKS)
                    nc.scalar.copy(agg[:, t, 0:D1], banks[t][:, 0:D1]).then_inc(tile_copied, 1)

            def finish(s):
                n, t0 = BLOCKS[s], FIRST[s]
                act.wait_ge(y_ready, s + 1)
                for t in range(n):
                    last = nc.scalar.activation(agg[:, t, 0:D], y[:, t, :], ACT.Identity, accum_out=total[:, t:t + 1])
                last.then_inc(total_ready, 1)
                act.wait_ge(mean_ready, s + 1)
                for t in range(n):
                    last = nc.scalar.activation(agg[:, t, 0:D], y[:, t, :], ACT.Square, bias=neg_mean[:, t:t + 1],
                                                accum_out=square_sum[:, t:t + 1])
                last.then_inc(squares_ready, 1)
                act.wait_ge(offset_ready, s + 1)
                for t in range(n):
                    last = nc.scalar.activation(y[:, t, :], y[:, t, :], ACT.Identity, bias=offset[:, t:t + 1],
                                                scale=rstd[:, t:t + 1])
                last.then_inc(out_ready, 1)
                act.wait_ge(out_ready, s + 1)
                act.dma_start(out_v[:, t0:t0 + n, :], y[:, 0:n, :]).then_inc(out_stored, 16)

            for t in range(FIRST[2]):
                to_bytes(t)
            for s in range(NB):
                copy_sums(s)
                ahead = range(FIRST[s + 2], FIRST[s + 2] + BLOCKS[s + 2]) if s + 2 < NB else []
                for t in ahead[:BYTE_SLOTS]:
                    to_bytes(t)
                finish(s)
                for t in ahead[BYTE_SLOTS:]:
                    to_bytes(t)
            act.wait_ge(out_stored, 16 * NB)

        @block.vector
        def _(dve):
            dve.wait_ge(attn_loaded, 32)
            dve.wait_ge(consts_ready, 1)
            nc.vector.tensor_scalar(attn_iw[:], ones[:], attn_i[:], None, ALU.mult).then_inc(attn_wide, 1)
            dve.wait_ge(x_loaded, 16 * Q * FB)
            nc.vector.tensor_tensor(prod.rearrange("p (c d) -> p c d", c=CHUNKS), xj[:, :, 0:D],
                                    attn_j[:].unsqueeze(1).broadcast_to([P, CHUNKS, D]),
                                    ALU.mult).then_inc(products_ready, 1)
            dve.wait_ge(products_ready, 1)
            nc.vector.reduce_sum(s_j[:], prod.rearrange("p (c d) -> p c d", c=CHUNKS), X).then_inc(s_j_ready, 1)
            dve.wait_ge(s_j_ready, 1)
            nc.vector.reduce_max(smax[:, 0:1], s_j[:], X).then_inc(row_max_ready, 1)
            dve.wait_ge(max_turned, 1)
            nc.vector.reduce_max(smax[0:1, 1:2], banks[7][0:1, 0:P], X).then_inc(max_found, 1)
            dve.wait_ge(max_spread, 1)
            nc.vector.tensor_scalar(shift[:, 0:1], banks[7][:, P:P + 1], SLOPE - 1, None, ALU.mult)
            nc.vector.tensor_scalar(shift[:, 1:2], banks[7][:, P:P + 1], -SLOPE, None, ALU.mult).then_inc(shift_ready, 1)
            dve.wait_ge(factors_ready, 1)
            nc.vector.tensor_tensor(xj[:, :, 0:D], xj[:, :, 0:D], d_j[:].unsqueeze(2).broadcast_to([P, CHUNKS, D]),
                                    ALU.mult).then_inc(xj_scaled, 1)
            dve.wait_ge(q_exp_ready, RB)
            nc.vector.tensor_scalar(q_row[:], q_row[:], 1.0, None, ALU.min).then_inc(q_ready, 1)

            def turn_mask(s, t):
                row = (t - FIRST[s]) * P
                dve.wait_ge(bytes_ready, t + 1)
                src = mask_bytes[:, t % BYTE_SLOTS, :, :].bitcast(u32).rearrange("p g (f w) -> p g f w", w=B)
                dst = mask_t[:, s % 2, :, :, :].rearrange("p f i k -> p f (i k)").bitcast(u32)
                nc.vector.transpose(dst[:, :, row:row + P].rearrange("p f (g a) -> p g f a", a=B),
                                    src).then_inc(mask_ready, 1)

            def finish(s):
                n, t0 = BLOCKS[s], FIRST[s]
                dve.wait_ge(tile_copied, t0 + n)
                nc.vector.reciprocal(rden[:, 0:n], agg[:, 0:n, D]).then_inc(rden_ready, 1)
                dve.wait_ge(rden_ready, s + 1)
                dve.wait_ge(xi_loaded, 16 * (s + 1))
                for t in range(n):
                    last = nc.vector.scalar_tensor_tensor(y[:, t, :], agg[:, t, 0:D], rden[:, t:t + 1],
                                                          y[:, t, :], ALU.mult, ALU.add)
                last.then_inc(y_ready, 1)

            dve.wait_ge(q_ready, 1)
            for t in range(BLOCKS[0]):
                turn_mask(0, t)
            for s in range(NB):
                n, t0 = BLOCKS[s], FIRST[s]
                dve.wait_ge(mask_ready, t0 + n)
                n_next = BLOCKS[s + 1] if s + 1 < NB else 0
                for f in range(FB):
                    for k in range(K):
                        c = f * K + k
                        g = s * CHUNKS + c
                        if g >= W_SLOTS:
                            dve.wait_ge(weights_used, g - W_SLOTS + 1)
                        nc.vector.scalar_tensor_tensor(
                            weights[:, k, 0:n * P], q_row[:, t0 * P:(t0 + n) * P], r_j[:, c:c + 1],
                            mask_t[:, s % 2, f, 0:n * P, k], ALU.max, ALU.mult).then_inc(weights_ready, 1)
                    if n_next >= FB // 2 and f % (FB // n_next) == FB // n_next - 1:
                        turn_mask(s + 1, FIRST[s + 1] + f // (FB // n_next))
                    if s >= 1 and f == 1:
                        finish(s - 1)
                if 0 < n_next < FB // 2:
                    for t in range(FIRST[s + 1], FIRST[s + 1] + n_next):
                        turn_mask(s + 1, t)
            finish(NB - 1)

        @block.tensor
        def _(pe):
            pe.wait_ge(consts_ready, 1)
            pe.wait_ge(x_loaded, 16 * Q * FB)
            for fb in range(FB):
                if fb >= 4:
                    pe.wait_ge(xT_ready, fb - 3)
                for k in range(K):
                    last = nc.tensor.transpose(banks[fb % 4][:, k * P:(k + 1) * P], xj[:, fb * K + k, 0:D], ident[:])
                last.then_inc(xT_in_psum, 1)
            pe.wait_ge(row_max_ready, 1)
            nc.tensor.transpose(banks[7][0:1, 0:P], smax[:, 0:1], ident[:]).then_inc(max_turned, 1)
            pe.wait_ge(max_found, 1)
            nc.tensor.matmul(banks[7][:, P:P + 1], ones[0:1, :], smax[0:1, 1:2], start=True, stop=True).then_inc(max_spread, 1)
            pe.wait_ge(attn_wide, 1)
            pe.wait_ge(xT_ready, FB)
            for rb in range(RB):
                if rb == RB - 1:
                    pe.wait_ge(q_exp_ready, 1)
                nc.tensor.matmul(banks[rb % (RB - 1)][:, :], attn_iw[:], xT[:, rb * BANK:(rb + 1) * BANK],
                                 start=True, stop=True).then_inc(s_i_in_psum, 1)
            pe.wait_ge(q_exp_ready, RB)
            pe.wait_ge(xj_scaled, 1)
            for s in range(NB):
                n, t0 = BLOCKS[s], FIRST[s]
                for c in range(CHUNKS):
                    pe.wait_ge(weights_ready, s * CHUNKS + c + 1)
                    for t in range(n):
                        if c == 0 and s >= 1 and t < BLOCKS[s - 1]:
                            pe.wait_ge(tile_copied, FIRST[s - 1] + t + 1)
                        last = nc.tensor.matmul(banks[t][:, 0:D1], weights[:, c % W_SLOTS, t * P:(t + 1) * P],
                                                xj[:, c, 0:D1], start=(c == 0), stop=(c == CHUNKS - 1))
                        if c == CHUNKS - 1 and t < n - 1:
                            last.then_inc(tile_summed, 1)
                    last.then_inc(weights_used, 1)


_INS = ['x', 'adj', 'L0_gnn_attn']


def kernel(**inputs):
    import numpy as _np
    import concourse.bacc as _bacc
    from concourse import mybir as _mybir
    from concourse.bass_utils import run_bass_kernel_spmd as _run

    nc = _bacc.Bacc("TRN2", target_bir_lowering=False, num_devices=1)
    arrays, args = {}, []
    for name in _INS:
        a = _np.ascontiguousarray(inputs[name])
        arrays[f"in_{name}_dram"] = a
        args.append(nc.dram_tensor(f"in_{name}_dram", a.shape, _mybir.dt.from_np(a.dtype), kind="ExternalInput").ap())
    args.append(nc.dram_tensor("out_0_dram", (4096, 128), _mybir.dt.float32, kind="ExternalOutput").ap())
    gat_kernel(nc, *args)
    r = _run(nc, [arrays], core_ids=[0])
    return r.results[0]["out_0_dram"]
```

```python
import concourse.bass as bass
from concourse import mybir
from contextlib import ExitStack



def gat_kernel(nc: bass.Bass, x: bass.AP, adj: bass.AP, attn: bass.AP, out: bass.AP):
    fp32 = mybir.dt.float32
    i32 = mybir.dt.int32
    u8 = mybir.dt.uint8
    u32 = mybir.dt.uint32
    ALU = mybir.AluOpType
    ACT = mybir.ActivationFunctionType
    X = mybir.AxisListType.X

    P = 128
    N, D = x.shape
    D1 = D + 1
    PITCH = D + 2
    Q = 4
    B = 32
    K = 4
    F = 2
    QC = F * B * K
    STRIPE = Q * QC
    STRIPES = N // STRIPE
    SC = F * K
    CHUNKS = STRIPES * SC
    T = 8
    ROWS = T * P
    BLOCKS = N // ROWS
    H = 2
    UROWS = ROWS // H
    G = UROWS // B
    UNITS = STRIPES * H
    ADJ_SLOTS = 4
    BYTE_SLOTS = 4
    W_SLOTS = 8
    LAST = 4
    GROUP = 2
    SLOPE = 0.2
    EPS = 1e-5
    BANK = 512
    RB = N // BANK
    S_I_BANK = [4, 5, 0, 1, 2, 3, 6, 7]

    adj_v = adj.rearrange("(u g a) (st q c) -> u st q a g c", g=G, a=B, q=Q, c=QC)
    xj_v = x.rearrange("(st q f b k) d -> q st b f (k d)", q=Q, f=F, b=B, k=K)
    xi_v = x.rearrange("(t p) d -> p t d", p=P)
    out_v = out.rearrange("(t p) d -> p t d", p=P)

    with ExitStack() as ctx:
        def sb(name, shape, dt):
            return ctx.enter_context(nc.sbuf_tensor(name, shape, dt))

        def sem(name):
            return ctx.enter_context(nc.semaphore(name))

        adj_in = sb("adj_in", [P, ADJ_SLOTS, G, QC], i32)
        mask_bytes = sb("mask_bytes", [P, BYTE_SLOTS, G, QC], u8)
        mask_t = sb("mask_t", [P, 2, F, ROWS, K], u8)
        weights = sb("weights", [P, W_SLOTS, ROWS], fp32)
        x_raw = sb("x_raw", [P, CHUNKS, D], fp32)
        xj = sb("xj", [P, CHUNKS, PITCH], fp32)
        q_row = sb("q_row", [P, N], fp32)
        prod = sb("prod", [P, CHUNKS, D], fp32)
        unused = sb("unused", [P, T, D], fp32)
        y = sb("y", [P, T, D], fp32)
        attn_i = sb("attn_i", [P, 1], fp32)
        attn_iw = sb("attn_iw", [P, P], fp32)
        attn_j = sb("attn_j", [P, D], fp32)
        ident = sb("ident", [P, P], fp32)
        ones = sb("ones", [P, P], fp32)
        s_j = sb("s_j", [P, CHUNKS], fp32)
        r_j = sb("r_j", [P, CHUNKS], fp32)
        d_j = sb("d_j", [P, CHUNKS], fp32)
        smax = sb("smax", [P, 2], fp32)
        shift = sb("shift", [P, 3], fp32)
        rden = sb("rden", [P, T], fp32)
        total = sb("total", [P, T], fp32)
        neg_mean = sb("neg_mean", [P, T], fp32)
        square_sum = sb("square_sum", [P, T], fp32)
        variance = sb("variance", [P, T], fp32)
        half = sb("half", [P, T], fp32)
        rstd = sb("rstd", [P, T], fp32)
        offset = sb("offset", [P, T], fp32)
        sig_bias = sb("sig_bias", [P, 1], fp32)

        xT = weights[:, 0:N // ROWS, :].rearrange("p w i -> p (w i)")

        banks = [ctx.enter_context(nc.psum_tensor(f"bank{i}", [P, BANK], fp32)) for i in range(8)]

        x_loaded = [sem(f"x_loaded{st}") for st in range(STRIPES)]
        attn_loaded = sem("attn_loaded")
        xi_loaded = sem("xi_loaded")
        adj_loaded = [sem(f"adj_loaded{i}") for i in range(ADJ_SLOTS)]
        out_stored = sem("out_stored")
        ident_zeroed = sem("ident_zeroed")
        consts_ready = sem("consts_ready")
        attn_wide = sem("attn_wide")
        xT_in_psum = sem("xT_in_psum")
        xT_ready = sem("xT_ready")
        s_i_in_psum = sem("s_i_in_psum")
        products_ready = sem("products_ready")
        s_j_ready = sem("s_j_ready")
        row_max_ready = sem("row_max_ready")
        max_turned = sem("max_turned")
        max_found = sem("max_found")
        max_spread = sem("max_spread")
        shift_ready = sem("shift_ready")
        factors_ready = sem("factors_ready")
        s_i_ready = sem("s_i_ready")
        q_ready = sem("q_ready")
        xj_scaled = sem("xj_scaled")
        bytes_ready = sem("bytes_ready")
        mask_ready = sem("mask_ready")
        weights_ready = sem("weights_ready")
        weights_used = sem("weights_used")
        tile_summed = sem("tile_summed")
        rden_ready = sem("rden_ready")
        y_ready = sem("y_ready")
        total_ready = sem("total_ready")
        mean_ready = sem("mean_ready")
        squares_ready = sem("squares_ready")
        variance_ready = sem("variance_ready")
        rstd_ready = sem("rstd_ready")
        offset_ready = sem("offset_ready")
        out_ready = sem("out_ready")

        block = ctx.enter_context(nc.Block())

        @block.sync
        def _(sp):
            sp.dma_start(attn_i[:], attn[0:D, :]).then_inc(attn_loaded, 16)
            sp.dma_start(attn_j[:], attn[D:2 * D, :].rearrange("d o -> o d").broadcast_to([P, D])).then_inc(attn_loaded, 16)
            for st in range(STRIPES):
                for q in range(Q):
                    sp.dma_start(x_raw[B * q:B * (q + 1), st * SC:(st + 1) * SC, :].rearrange("b (f k) d -> b f (k d)", f=F),
                                 xj_v[q, st, :, :, :]).then_inc(x_loaded[st], 16)

            def load_unit(ib, u):
                for q in range(Q):
                    sp.dma_start(adj_in[B * q:B * (q + 1), u % ADJ_SLOTS, :, :],
                                 adj_v[bass.ds(ib * H + u % H, 1), u // H, q, :, :, :].rearrange("o a g c -> (o a) g c")
                                 ).then_inc(adj_loaded[u % ADJ_SLOTS], 16)

            for u in range(ADJ_SLOTS):
                load_unit(0, u)
            for u in range(ADJ_SLOTS, UNITS):
                sp.wait_ge(bytes_ready, u - ADJ_SLOTS + 1)
                load_unit(0, u)
            with sp.Fori(1, BLOCKS) as ib:
                for u in range(UNITS):
                    sp.wait_ge(bytes_ready, ib * UNITS + (u - ADJ_SLOTS + 1))
                    load_unit(ib, u)

        @block.gpsimd
        def _(pool):
            nc.gpsimd.memset(ident[:], 0.0).then_inc(ident_zeroed, 1)
            nc.gpsimd.memset(ones[:], 1.0)
            nc.gpsimd.memset(half[:], -0.5)
            nc.gpsimd.memset(sig_bias[:], -100.0)
            pool.wait_ge(ident_zeroed, 1)
            nc.gpsimd.affine_select(out=ident[:], in_=ident[:], compare_op=ALU.not_equal, fill=1.0, base=0,
                                    pattern=[[-1, P]], channel_multiplier=1).then_inc(consts_ready, 1)

            def load_xi(ib):
                nc.gpsimd.dma_start(y[:], xi_v[:, bass.ds(ib * T, T), :]).then_inc(xi_loaded, 16)

            def statistics(call, t0, n):
                g = slice(t0, t0 + n)
                pool.wait_ge(total_ready, call + 1)
                nc.gpsimd.tensor_scalar(neg_mean[:, g], total[:, g], -1.0 / D, 0.0,
                                        ALU.mult, ALU.add).then_inc(mean_ready, 1)
                pool.wait_ge(squares_ready, call + 1)
                nc.gpsimd.tensor_scalar(variance[:, g], square_sum[:, g], 1.0 / D, EPS,
                                        ALU.mult, ALU.add).then_inc(variance_ready, 1)
                pool.wait_ge(variance_ready, call + 1)
                nc.gpsimd.tensor_tensor(rstd[:, g], variance[:, g], half[:, g], ALU.pow).then_inc(rstd_ready, 1)
                pool.wait_ge(rstd_ready, call + 1)
                nc.gpsimd.tensor_tensor(offset[:, g], neg_mean[:, g], rstd[:, g], ALU.mult).then_inc(offset_ready, 1)

            load_xi(0)
            for ib in range(BLOCKS - 1):
                statistics(ib, 0, T)
                pool.wait_ge(out_stored, 16 * (ib + 1))
                load_xi(ib + 1)
            for g in range(T // GROUP):
                statistics(BLOCKS - 1 + g, g * GROUP, GROUP)

        @block.scalar
        def _(act):
            xT_v = xT.rearrange("d (st q f b k) -> d st f k q b", q=Q, f=F, b=B, k=K)
            for m in range(CHUNKS // K):
                act.wait_ge(xT_in_psum, m + 1)
                nc.scalar.copy(xT_v[:, m // F, m % F, :, :, :],
                               banks[m % 4][:, :].rearrange("d (k q b) -> d k q b", k=K, q=Q)).then_inc(xT_ready, 1)
            act.wait_ge(shift_ready, 1)
            nc.scalar.activation(d_j[:], s_j[:], ACT.Exp, bias=shift[:, 1:2], scale=SLOPE).then_inc(factors_ready, 1)
            nc.scalar.activation(r_j[:], s_j[:], ACT.Exp, bias=shift[:, 0:1], scale=1 - SLOPE)
            nc.scalar.activation(xj[:, :, D], s_j[:], ACT.Exp, bias=shift[:, 1:2], scale=SLOPE)

            def q_factors(first, last, pieces):
                act.wait_ge(s_i_ready, pieces)
                nc.scalar.activation(q_row[:, first:last], q_row[:, first:last], ACT.Exp,
                                     bias=shift[:, 0:1], scale=SLOPE - 1).then_inc(q_ready, 1)

            q_factors(0, ROWS, ROWS // BANK)

            def to_bytes(ib, st, first=False):
                for h in range(H):
                    u = st * H + h
                    act.wait_ge(adj_loaded[u % ADJ_SLOTS], 16 * Q * (ib * (UNITS // ADJ_SLOTS) + u // ADJ_SLOTS + 1))
                    if not first:
                        act.wait_ge(mask_ready, ib * UNITS + (u - BYTE_SLOTS + 1))
                    nc.scalar.activation(mask_bytes[:, u % BYTE_SLOTS, :, :], adj_in[:, u % ADJ_SLOTS, :, :],
                                         ACT.Sigmoid, bias=sig_bias[:], scale=200.0).then_inc(bytes_ready, 1)

            def sum_rows(call, ib, t0, n):
                act.wait_ge(y_ready, ib * T + (t0 + n))
                for t in range(t0, t0 + n):
                    last = nc.scalar.activation(unused[:, t, :], y[:, t, :], ACT.Identity, accum_out=total[:, t:t + 1])
                last.then_inc(total_ready, 1)

            def sum_squares(call, t0, n):
                act.wait_ge(mean_ready, call + 1)
                for t in range(t0, t0 + n):
                    last = nc.scalar.activation(unused[:, t, :], y[:, t, :], ACT.Square, bias=neg_mean[:, t:t + 1],
                                                accum_out=square_sum[:, t:t + 1])
                last.then_inc(squares_ready, 1)

            def normalise(call, ib, t0, n):
                act.wait_ge(offset_ready, call + 1)
                for t in range(t0, t0 + n):
                    last = nc.scalar.activation(y[:, t, :], y[:, t, :], ACT.Identity, bias=offset[:, t:t + 1],
                                                scale=rstd[:, t:t + 1])
                last.then_inc(out_ready, 1)
                act.wait_ge(out_ready, call + 1)
                act.dma_start(out_v[:, bass.ds(ib * T + t0, n), :], y[:, t0:t0 + n, :]).then_inc(out_stored, 16)

            to_bytes(0, 0, first=True)
            to_bytes(0, 1, first=True)
            q_factors(ROWS, N, RB)
            to_bytes(0, 2)
            to_bytes(0, 3)
            with act.Fori(1, BLOCKS) as ib:
                to_bytes(ib, 0)
                to_bytes(ib, 1)
                sum_rows(ib - 1, ib - 1, 0, T)
                to_bytes(ib, 2)
                sum_squares(ib - 1, 0, T)
                to_bytes(ib, 3)
                normalise(ib - 1, ib - 1, 0, T)
            ib = BLOCKS - 1
            for g in range(T // GROUP):
                sum_rows(ib + g, ib, g * GROUP, GROUP)
                sum_squares(ib + g, g * GROUP, GROUP)
                normalise(ib + g, ib, g * GROUP, GROUP)
            act.wait_ge(out_stored, 16 * (ib + T // GROUP))

        @block.vector
        def _(dve):
            dve.wait_ge(attn_loaded, 32)
            dve.wait_ge(consts_ready, 1)
            nc.vector.tensor_scalar(attn_iw[:], ones[:], attn_i[:], None, ALU.mult).then_inc(attn_wide, 1)
            for st in range(STRIPES + 1):
                if st < STRIPES:
                    dve.wait_ge(x_loaded[st], 16 * Q)
                    c = slice(st * SC, (st + 1) * SC)
                    nc.vector.tensor_tensor(prod[:, c, :], x_raw[:, c, :], attn_j[:].unsqueeze(1).broadcast_to([P, SC, D]),
                                            ALU.mult).then_inc(products_ready, 1)
                if st >= 1:
                    c = slice((st - 1) * SC, st * SC)
                    dve.wait_ge(products_ready, st)
                    nc.vector.reduce_sum(s_j[:, c], prod[:, c, :], X).then_inc(s_j_ready, 1)
            dve.wait_ge(s_j_ready, STRIPES)
            nc.vector.reduce_max(smax[:, 0:1], s_j[:], X).then_inc(row_max_ready, 1)
            dve.wait_ge(max_turned, 1)
            nc.vector.reduce_max(smax[0:1, 1:2], banks[7][0:1, 0:P], X).then_inc(max_found, 1)
            dve.wait_ge(max_spread, 1)
            nc.vector.tensor_scalar(shift[:, 0:1], banks[7][:, P:P + 1], SLOPE - 1, None, ALU.mult)
            nc.vector.tensor_scalar(shift[:, 1:2], banks[7][:, P:P + 1], -SLOPE, None, ALU.mult)
            nc.vector.tensor_scalar(shift[:, 2:3], banks[7][:, P:P + 1], -1.0, None, ALU.mult).then_inc(shift_ready, 1)
            dve.wait_ge(shift_ready, 1)

            def s_i_piece(rb):
                dve.wait_ge(s_i_in_psum, rb + 1)
                nc.vector.tensor_scalar(q_row[:, rb * BANK:(rb + 1) * BANK], banks[S_I_BANK[rb]][:, :],
                                        shift[:, 2:3], None, ALU.max).then_inc(s_i_ready, 1)

            def scale_xj(st):
                c = slice(st * SC, (st + 1) * SC)
                nc.vector.tensor_tensor(xj[:, c, 0:D], x_raw[:, c, :], d_j[:, c].unsqueeze(2).broadcast_to([P, SC, D]),
                                        ALU.mult).then_inc(xj_scaled, 1)

            for rb in range(ROWS // BANK):
                s_i_piece(rb)
            dve.wait_ge(factors_ready, 1)
            scale_xj(0)
            for rb in range(ROWS // BANK, RB):
                s_i_piece(rb)

            def turn_unit(ib, st, h):
                u = st * H + h
                dve.wait_ge(bytes_ready, ib * UNITS + (u + 1))
                src = mask_bytes[:, u % BYTE_SLOTS, :, :].bitcast(u32).rearrange("p g (f w) -> p g f w", w=B)
                dst = mask_t[:, st % 2, :, :, :].rearrange("p f i k -> p f (i k)").bitcast(u32)
                nc.vector.transpose(dst[:, :, h * UROWS:(h + 1) * UROWS].rearrange("p f (g a) -> p g f a", a=B),
                                    src).then_inc(mask_ready, 1)

            def residual(ib):
                dve.wait_ge(xi_loaded, 16 * ib + 16)
                for t in range(T):
                    if t < T - 1:
                        dve.wait_ge(tile_summed, ib * (T - 1) + (t + 1))
                    else:
                        dve.wait_ge(weights_used, ib * CHUNKS + CHUNKS)
                    nc.vector.reciprocal(rden[:, t:t + 1], banks[t][:, D:D1]).then_inc(rden_ready, 1)
                    dve.wait_ge(rden_ready, ib * T + (t + 1))
                    nc.vector.scalar_tensor_tensor(y[:, t, :], banks[t][:, 0:D], rden[:, t:t + 1],
                                                   y[:, t, :], ALU.mult, ALU.add).then_inc(y_ready, 1)

            def weigh(ib, c, rows, first=False):
                if not first or c >= W_SLOTS:
                    dve.wait_ge(weights_used, ib * CHUNKS + (c - W_SLOTS + 1))
                nc.vector.scalar_tensor_tensor(
                    weights[:, c % W_SLOTS, rows], q_row[:, bass.ds(ib * ROWS + rows.start, rows.stop - rows.start)],
                    r_j[:, c:c + 1], mask_t[:, c // SC % 2, c % SC // K, rows, c % K],
                    ALU.max, ALU.mult).then_inc(weights_ready, 1)

            def stripe(ib, st, first=False, final=False):
                dve.wait_ge(mask_ready, ib * UNITS + (st + 1) * H)
                for s in range(SC):
                    c = st * SC + s
                    weigh(ib, c, slice(0, ROWS), first)
                    if s % (SC // H) == 1 and not (final and st == STRIPES - 1):
                        dve.wait_ge(weights_ready, ib * CHUNKS + (st * SC + SC))
                        if st + 1 < STRIPES:
                            turn_unit(ib, st + 1, s // (SC // H))
                        else:
                            turn_unit(ib + 1, 0, s // (SC // H))
                    if first and s == 2 and st + 1 < STRIPES:
                        scale_xj(st + 1)
                    if first and st == 2 and s == 0:
                        dve.wait_ge(q_ready, 2)
                    if not first and c == LAST - 1:
                        residual(ib - 1)

            for h in range(H):
                turn_unit(0, 0, h)
                if h == 0:
                    dve.wait_ge(q_ready, 1)
                dve.wait_ge(mask_ready, h + 1)
                for c in range(SC):
                    weigh(0, c, slice(h * UROWS, (h + 1) * UROWS), first=True)
            scale_xj(1)
            for h in range(H):
                turn_unit(0, 1, h)
            for st in range(1, STRIPES):
                stripe(0, st, first=True)
            with dve.Fori(1, BLOCKS - 1) as ib:
                for st in range(STRIPES):
                    stripe(ib, st)
            for st in range(STRIPES):
                stripe(BLOCKS - 1, st, final=True)
            residual(BLOCKS - 1)

        @block.tensor
        def _(pe):
            pe.wait_ge(consts_ready, 1)
            for m in range(CHUNKS // K):
                if m % F == 0:
                    pe.wait_ge(x_loaded[m // F], 16 * Q)
                if m >= 4:
                    pe.wait_ge(xT_ready, m - 3)
                for k in range(K):
                    last = nc.tensor.transpose(banks[m % 4][:, k * P:(k + 1) * P], x_raw[:, m * K + k, :], ident[:])
                last.then_inc(xT_in_psum, 1)

            def s_i_piece(rb):
                nc.tensor.matmul(banks[S_I_BANK[rb]][:, :], attn_iw[:], xT[:, rb * BANK:(rb + 1) * BANK],
                                 start=True, stop=True).then_inc(s_i_in_psum, 1)

            pe.wait_ge(attn_wide, 1)
            pe.wait_ge(xT_ready, CHUNKS // K)
            for rb in range(ROWS // BANK):
                s_i_piece(rb)
            pe.wait_ge(row_max_ready, 1)
            nc.tensor.transpose(banks[7][0:1, 0:P], smax[:, 0:1], ident[:]).then_inc(max_turned, 1)
            pe.wait_ge(max_found, 1)
            nc.tensor.matmul(banks[7][:, P:P + 1], ones[0:1, :], smax[0:1, 1:2], start=True, stop=True).then_inc(max_spread, 1)
            for rb in range(ROWS // BANK, RB):
                if S_I_BANK[rb] == 7:
                    pe.wait_ge(shift_ready, 1)
                s_i_piece(rb)
            pe.wait_ge(s_i_ready, RB)

            def product(c, t):
                return nc.tensor.matmul(banks[t][:, 0:D1], weights[:, c % W_SLOTS, t * P:(t + 1) * P],
                                        xj[:, c, 0:D1], start=(c == 0), stop=(c == CHUNKS - 1))

            def row_block(ib, first=False):
                for c in range(SC if first else 0, CHUNKS - LAST):
                    if first and c % SC == 0:
                        pe.wait_ge(xj_scaled, c // SC + 1)
                    pe.wait_ge(weights_ready, ib * CHUNKS + (SC + c + 1))
                    for t in range(T):
                        if c == 0:
                            pe.wait_ge(y_ready, (ib - 1) * T + (t + 1))
                        last = product(c, t)
                    last.then_inc(weights_used, 1)
                pe.wait_ge(weights_ready, ib * CHUNKS + (SC + CHUNKS))
                for t in range(T):
                    for c in range(CHUNKS - LAST, CHUNKS):
                        last = product(c, t)
                        if t == T - 1:
                            last.then_inc(weights_used, 1)
                    if t < T - 1:
                        last.then_inc(tile_summed, 1)

            pe.wait_ge(xj_scaled, 1)
            for h in range(H):
                for c in range(SC):
                    pe.wait_ge(weights_ready, h * SC + c + 1)
                    for t in range(h * T // H, (h + 1) * T // H):
                        last = product(c, t)
                    if h == H - 1:
                        last.then_inc(weights_used, 1)
            row_block(0, first=True)
            with pe.Fori(1, BLOCKS) as ib:
                row_block(ib)


_INS = ['x', 'adj', 'L0_gnn_attn']


def kernel(**inputs):
    import numpy as _np
    import concourse.bacc as _bacc
    from concourse import mybir as _mybir
    from concourse.bass_utils import run_bass_kernel_spmd as _run

    nc = _bacc.Bacc("TRN2", target_bir_lowering=False, num_devices=1)
    arrays, args = {}, []
    for name in _INS:
        a = _np.ascontiguousarray(inputs[name])
        arrays[f"in_{name}_dram"] = a
        args.append(nc.dram_tensor(f"in_{name}_dram", a.shape, _mybir.dt.from_np(a.dtype), kind="ExternalInput").ap())
    args.append(nc.dram_tensor("out_0_dram", (4096, 128), _mybir.dt.float32, kind="ExternalOutput").ap())
    gat_kernel(nc, *args)
    r = _run(nc, [arrays], core_ids=[0])
    return r.results[0]["out_0_dram"]
```

```python
import concourse.bass as bass
from concourse import mybir
from contextlib import ExitStack



def gat_kernel(nc: bass.Bass, x: bass.AP, adj: bass.AP, attn: bass.AP, out: bass.AP):
    fp32 = mybir.dt.float32
    i32 = mybir.dt.int32
    u8 = mybir.dt.uint8
    u32 = mybir.dt.uint32
    ALU = mybir.AluOpType
    ACT = mybir.ActivationFunctionType
    X = mybir.AxisListType.X

    P = 128
    N, D = x.shape
    D1 = D + 1
    PITCH = D + 2
    Q = 4
    B = 32
    K = 4
    F = 2
    QC = F * B * K
    STRIPE = Q * QC
    STRIPES = N // STRIPE
    SC = F * K
    CHUNKS = STRIPES * SC
    TILES = N // P
    T = 8
    ROWS = T * P
    BLOCKS = N // ROWS
    H = 2
    UROWS = ROWS // H
    G = UROWS // B
    UNITS = STRIPES * H
    ADJ_SLOTS = 4
    BYTE_SLOTS = 4
    W_SLOTS = 8
    TURN_AT = [4, 7]
    FIRST_TURNS = {(0, 1, 6): (1, 0), (1, 0, 4): (1, 1), (1, 1, 4): (2, 0), (2, 0, 4): (2, 1),
                   (2, 1, 4): (3, 0), (3, 0, 4): (3, 1)}
    LAST = 6
    RESIDUAL_AT = 1
    GROUPS = [slice(0, T // 2), slice(T // 2, T)]
    LAST_GROUPS = [slice(0, 2), slice(2, 4), slice(4, 6), slice(6, 7), slice(7, 8)]
    SLOPE = 0.2
    EPS = 1e-5
    NEG_INF = -1e9
    LEAST = 1e-37
    MOST = 1e28
    BANK = 512
    RB = N // BANK
    S_J_BY_ACT = 1
    EARLY = len(LAST_GROUPS) - 2
    XT_BANK = 4
    S_BANK = 3
    S_I_BANK = [0, 1, 2, 4, 5, 6, 7, S_BANK]
    WARM = 14
    KEEP_WARM = 22

    adj_v = adj.rearrange("(u g a) (st q c) -> u st q a g c", g=G, a=B, q=Q, c=QC)
    xj_v = x.rearrange("(st q f b k) d -> q st b f (k d)", q=Q, f=F, b=B, k=K)
    xi_v = x.rearrange("(t p) d -> p t d", p=P)
    out_v = out.rearrange("(t p) d -> p t d", p=P)

    with ExitStack() as ctx:
        def sb(name, shape, dt):
            return ctx.enter_context(nc.sbuf_tensor(name, shape, dt))

        def sem(name):
            return ctx.enter_context(nc.semaphore(name))

        adj_in = sb("adj_in", [P, ADJ_SLOTS, G, QC], i32)
        mask_bytes = sb("mask_bytes", [P, BYTE_SLOTS, G, QC], u8)
        mask_t = sb("mask_t", [P, 2, F, ROWS, K], u8)
        weights = sb("weights", [P, W_SLOTS, ROWS], fp32)
        x_raw = sb("x_raw", [P, CHUNKS, D], fp32)
        xj = sb("xj", [P, CHUNKS, PITCH], fp32)
        q_row = sb("q_row", [P, N], fp32)
        prod = sb("prod", [P, CHUNKS, D], fp32)
        unused = sb("unused", [P, T, D], fp32)
        y = sb("y", [P, 2, D], fp32)
        attn_i = sb("attn_i", [P, 1], fp32)
        attn_iw = sb("attn_iw", [P, P], fp32)
        attn_j = sb("attn_j", [P, D], fp32)
        ident = sb("ident", [P, P], fp32)
        ones = sb("ones", [P, P], fp32)
        s_j = sb("s_j", [P, CHUNKS], fp32)
        r_j = sb("r_j", [P, CHUNKS], fp32)
        d_j = sb("d_j", [P, CHUNKS], fp32)
        smax = sb("smax", [P, 2], fp32)
        shift = sb("shift", [P, 3], fp32)
        rden = sb("rden", [P, T], fp32)
        total = sb("total", [P, T], fp32)
        neg_mean = sb("neg_mean", [P, T], fp32)
        square_sum = sb("square_sum", [P, T], fp32)
        variance = sb("variance", [P, T], fp32)
        half = sb("half", [P, T], fp32)
        rstd = sb("rstd", [P, T], fp32)
        half_moments = sb("half_moments", [P, T, 6], fp32)
        moments = sb("moments", [P, T, 2], fp32)
        deviations = sb("deviations", [P, T], fp32)
        offset = sb("offset", [P, T], fp32)
        carried = sb("carried", [P, 3], fp32)
        sig_bias = sb("sig_bias", [P, 1], fp32)

        worst = sb("worst", [P, T + 2], fp32)
        again = sb("again", [1, 1], i32)
        attn_col = sb("attn_col", [P, 1], fp32)
        attn_row = sb("attn_row", [P, D], fp32)
        s_i = sb("s_i", [P, TILES], fp32)
        neg_max = sb("neg_max", [P, 2], fp32)
        den = sb("den", [P, 2], fp32)
        deviation = sb("deviation", [P, 2], fp32)
        eps = sb("eps", [P, 1], fp32)

        xT_slot = W_SLOTS - N // ROWS
        xT = weights[:, xT_slot:, :].rearrange("p w i -> p (w i)")
        xi = prod

        def tile(t):
            return xi[:, bass.ds(t, 1), :].rearrange("p o d -> p (o d)")

        rows = adj_in[:, :, :, :].rearrange("p s g c -> p s (g c)")
        adj_rows = rows[:, 0, :]
        scores = rows[:, 1, :].bitcast(fp32)
        leaky = rows[:, 2, :].bitcast(fp32)
        turned = rows[:, 3, :].bitcast(fp32)
        s_j_row = q_row

        psum = ctx.enter_context(nc.psum_tensor("psum", [P, 8, BANK], fp32))
        banks = [psum[:, i, :] for i in range(8)]

        x_loaded = [sem(f"x_loaded{st}") for st in range(STRIPES)]
        attn_j_loaded = sem("attn_j_loaded")
        attn_loaded = sem("attn_loaded")
        first_half_loaded = sem("first_half_loaded")
        adj_loaded = [sem(f"adj_loaded{i}") for i in range(ADJ_SLOTS)]
        first_xi_loaded = sem("first_xi_loaded")
        xi_loaded = sem("xi_loaded")
        stored = sem("stored")
        ident_zeroed = sem("ident_zeroed")
        consts_ready = sem("consts_ready")
        attn_wide = sem("attn_wide")
        xT_in_psum = sem("xT_in_psum")
        xT_ready = sem("xT_ready")
        s_i_in_psum = sem("s_i_in_psum")
        products_ready = sem("products_ready")
        s_j_ready = sem("s_j_ready")
        s_j_by_act_ready = sem("s_j_by_act_ready")
        first_bytes_ready = sem("first_bytes_ready")
        row_max_ready = sem("row_max_ready")
        max_turned = sem("max_turned")
        max_found = sem("max_found")
        max_spread = sem("max_spread")
        shift_ready = sem("shift_ready")
        factors_ready = sem("factors_ready")
        s_i_ready = sem("s_i_ready")
        q_ready = sem("q_ready")
        first_xj_scaled = sem("first_xj_scaled")
        xj_scaled = sem("xj_scaled")
        bytes_ready = sem("bytes_ready")
        mask_ready = sem("mask_ready")
        weights_ready = sem("weights_ready")
        weights_used = sem("weights_used")
        tile_summed = sem("tile_summed")
        den_ready = sem("den_ready")
        rden_ready = sem("rden_ready")
        y_ready = sem("y_ready")
        total_ready = sem("total_ready")
        mean_ready = sem("mean_ready")
        squares_ready = sem("squares_ready")
        half_moments_ready = sem("half_moments_ready")
        moments_ready = sem("moments_ready")
        last_deviation_ready = sem("last_deviation_ready")
        last_rstd_ready = sem("last_rstd_ready")
        early_out_ready = sem("early_out_ready")
        last_out_ready = sem("last_out_ready")
        last_stored = sem("last_stored")
        variance_ready = sem("variance_ready")
        rstd_ready = sem("rstd_ready")
        offset_ready = sem("offset_ready")
        out_ready = sem("out_ready")

        worst_ready = sem("worst_ready")
        worst_turned = sem("worst_turned")
        worst_found = sem("worst_found")
        again_ready = sem("again_ready")
        inputs_again = sem("inputs_again")
        wide_again = sem("wide_again")
        x_turned = sem("x_turned")
        x_turned_ready = sem("x_turned_ready")
        s_j_in_psum = sem("s_j_in_psum")
        s_j_row_ready = sem("s_j_row_ready")
        s_i_products = sem("s_i_products")
        adj_rows_free = sem("adj_rows_free")
        adj_rows_loaded = sem("adj_rows_loaded")
        score_step = sem("score_step")
        scores_ready = sem("scores_ready")
        probs_ready = sem("probs_ready")
        probs_turned = sem("probs_turned")
        turned_ready = sem("turned_ready")
        sum_ready = sem("sum_ready")
        row_step = sem("row_step")
        mean_again = sem("mean_again")
        squares_again = sem("squares_again")
        deviation_ready = sem("deviation_ready")
        scale_ready = sem("scale_ready")
        row_out_ready = sem("row_out_ready")
        row_stored = sem("row_stored")

        block = ctx.enter_context(nc.Block())

        @block.sync
        def _(sp):
            for st in range(STRIPES):
                for q in range(Q):
                    sp.dma_start(x_raw[B * q:B * (q + 1), st * SC:(st + 1) * SC, :].rearrange("b (f k) d -> b f (k d)", f=F),
                                 xj_v[q, st, :, :, :]).then_inc(x_loaded[st], 16)

            def load_unit(ib, u):
                for q in range(Q):
                    sp.dma_start(adj_in[B * q:B * (q + 1), u % ADJ_SLOTS, :, :],
                                 adj_v[bass.ds(ib * H + u % H, 1), u // H, q, :, :, :].rearrange("o a g c -> (o a) g c")
                                 ).then_inc(adj_loaded[u % ADJ_SLOTS], 16)

            for g, loaded in ((slice(0, G // 2), first_half_loaded), (slice(G // 2, G), adj_loaded[0])):
                for q in range(Q):
                    sp.dma_start(adj_in[B * q:B * (q + 1), 0, g, :], adj_v[0, 0, q, :, g, :]).then_inc(loaded, 16)
            for u in range(1, ADJ_SLOTS):
                load_unit(0, u)
            for u in range(ADJ_SLOTS, UNITS):
                if u == ADJ_SLOTS:
                    sp.wait_ge(first_bytes_ready, 2)
                else:
                    sp.wait_ge(bytes_ready, u - ADJ_SLOTS)
                load_unit(0, u)
            sp.wait_ge(row_max_ready, 1)
            sp.dma_start(xi[:, 0:T, :], xi_v[:, 0:T, :]).then_inc(first_xi_loaded, 16)

            def load_block(ib):
                for u in range(UNITS):
                    sp.wait_ge(bytes_ready, ib * UNITS + (u - ADJ_SLOTS))
                    load_unit(ib, u)

            load_block(1)
            sp.dma_start(xi[:, T:, :], xi_v[:, T:, :]).then_inc(xi_loaded, 16)
            with sp.Fori(2, BLOCKS) as ib:
                load_block(ib)

            for g, v in enumerate(LAST_GROUPS):
                if g < EARLY:
                    sp.wait_ge(early_out_ready, g + 1)
                else:
                    sp.wait_ge(last_out_ready, g - EARLY + 1)
                sp.dma_start(out_v[:, (BLOCKS - 1) * T + v.start:(BLOCKS - 1) * T + v.stop, :],
                             xi[:, (BLOCKS - 1) * T + v.start:(BLOCKS - 1) * T + v.stop, :]).then_inc(last_stored, 16)
            sp.wait_ge(last_stored, 16 * len(LAST_GROUPS))

            sp.wait_ge(again_ready, 1)
            with sp.If(sp.value_load(again[0:1, 0:1], min_val=0, max_val=1) > 0):
                sp.wait_ge(stored, 16 * (BLOCKS - 1))
                sp.dma_start(xi[:], xi_v).then_inc(inputs_again, 16)
                sp.dma_start(attn_col[:], attn[D:2 * D, :]).then_inc(inputs_again, 16)
                sp.dma_start(attn_row[:], attn[0:D, :].rearrange("d o -> o d").broadcast_to([P, D])).then_inc(inputs_again, 16)
                with sp.Fori(0, TILES) as t:
                    sp.wait_ge(adj_rows_free, t + 1)
                    sp.dma_start(adj_rows, adj[bass.ds(t * P, P), :]).then_inc(adj_rows_loaded, 16)

        @block.gpsimd
        def _(pool):
            nc.gpsimd.memset(ident[:], 0.0).then_inc(ident_zeroed, 1)
            nc.gpsimd.memset(ones[:], 1.0)
            nc.gpsimd.memset(half[:], -0.5)
            nc.gpsimd.memset(sig_bias[:], -100.0)
            nc.gpsimd.memset(eps[:], EPS)
            nc.gpsimd.memset(worst[:], 0.0).then_inc(worst_ready, 1)
            pool.wait_ge(ident_zeroed, 1)
            nc.gpsimd.affine_select(out=ident[:], in_=ident[:], compare_op=ALU.not_equal, fill=1.0, base=0,
                                    pattern=[[-1, P]], channel_multiplier=1).then_inc(consts_ready, 1)
            pool.dma_start(attn_j[:], attn[D:2 * D, :].rearrange("d o -> o d").broadcast_to([P, D])
                           ).then_inc(attn_j_loaded, 16)
            pool.dma_start(attn_i[:], attn[0:D, :]).then_inc(attn_loaded, 16)

            for ib in range(BLOCKS - 1):
                pool.wait_ge(total_ready, ib + 1)
                nc.gpsimd.tensor_scalar(neg_mean[:], total[:], -1.0 / D, 0.0, ALU.mult, ALU.add).then_inc(mean_ready, 1)
                pool.wait_ge(squares_ready, ib + 1)
                nc.gpsimd.tensor_scalar(variance[:], square_sum[:], 1.0 / D, EPS, ALU.mult, ALU.add).then_inc(variance_ready, 1)
                pool.wait_ge(variance_ready, ib + 1)
                nc.gpsimd.tensor_tensor(rstd[:], variance[:], half[:], ALU.pow).then_inc(rstd_ready, 1)
                pool.wait_ge(rstd_ready, ib + 1)
                nc.gpsimd.tensor_tensor(offset[:], neg_mean[:], rstd[:], ALU.mult).then_inc(offset_ready, 1)
            pool.wait_ge(out_ready, BLOCKS - 1)
            for g, v in enumerate(LAST_GROUPS[:EARLY]):
                pool.wait_ge(moments_ready, v.stop)
                nc.gpsimd.tensor_scalar(variance[:, v], moments[:, v, 1], 1.0, EPS,
                                        ALU.mult, ALU.add)
                nc.gpsimd.tensor_scalar(neg_mean[:, v], moments[:, v, 0], -1.0, 0.0,
                                        ALU.mult, ALU.add).then_inc(variance_ready, 1)
                pool.wait_ge(variance_ready, BLOCKS + g)
                nc.gpsimd.tensor_tensor(rstd[:, v], variance[:, v], half[:, v], ALU.pow).then_inc(rstd_ready, 1)
                pool.wait_ge(rstd_ready, BLOCKS + g)
                nc.gpsimd.tensor_tensor(offset[:, v], neg_mean[:, v], rstd[:, v], ALU.mult).then_inc(offset_ready, 1)

        @block.scalar
        def _(act):
            for m in range(CHUNKS // K):
                act.wait_ge(xT_in_psum, m + 1)
                nc.scalar.copy(xT[:, m * BANK:(m + 1) * BANK], banks[XT_BANK + m % 4][:, :]).then_inc(xT_ready, 1)
                if m == 2:
                    act.wait_ge(products_ready, S_J_BY_ACT + 1)
                    for s in range(SC):
                        c = S_J_BY_ACT * SC + s
                        last = nc.scalar.activation(unused[:, s, :], prod[:, c, :], ACT.Identity, accum_out=s_j[:, c:c + 1])
                    last.then_inc(s_j_by_act_ready, 1)
            act.wait_ge(shift_ready, 1)
            nc.scalar.activation(d_j[:], s_j[:], ACT.Exp, bias=shift[:, 1:2], scale=SLOPE).then_inc(factors_ready, 1)
            nc.scalar.activation(r_j[:], s_j[:], ACT.Exp, bias=shift[:, 0:1], scale=1 - SLOPE)
            nc.scalar.activation(xj[:, :, D], s_j[:], ACT.Exp, bias=shift[:, 1:2], scale=SLOPE)

            q_row_v = q_row[:, :].rearrange("p (st q f b k) -> p st f k q b", q=Q, f=F, b=B, k=K)

            def s_i_piece(rb):
                act.wait_ge(s_i_in_psum, rb + 1)
                nc.scalar.activation(q_row_v[:, rb // F, rb % F, :, :, :],
                                     banks[S_I_BANK[rb]][:, :].rearrange("p (k q b) -> p k q b", k=K, q=Q),
                                     ACT.Relu, bias=shift[:, 2:3]).then_inc(s_i_ready, 1)

            def q_factors(first, last):
                nc.scalar.activation(q_row[:, first:last], q_row[:, first:last], ACT.Exp,
                                     scale=SLOPE - 1).then_inc(q_ready, 1)

            for rb in range(ROWS // BANK):
                s_i_piece(rb)
            act.wait_ge(s_i_ready, ROWS // BANK)
            q_factors(0, UROWS)
            for rb in (2, 7):
                s_i_piece(rb)
            q_factors(UROWS, ROWS)
            for rb in (3, 4):
                s_i_piece(rb)

            def scale_xj(st):
                for c in range(st * SC, (st + 1) * SC):
                    last = nc.scalar.activation(xj[:, c, 0:D], x_raw[:, c, :], ACT.Copy, scale=d_j[:, c:c + 1])
                last.then_inc(xj_scaled, 1)

            def to_bytes(ib, st, first=False):
                for h in range(H):
                    u = st * H + h
                    if first and u == 0:
                        continue
                    if first and u == 2:
                        s_i_piece(5)
                        s_i_piece(6)
                    act.wait_ge(adj_loaded[u % ADJ_SLOTS], 16 * Q * (ib * (UNITS // ADJ_SLOTS) + u // ADJ_SLOTS + 1))
                    if not first or u >= BYTE_SLOTS:
                        act.wait_ge(mask_ready, ib * UNITS + (u - BYTE_SLOTS + 1))
                    nc.scalar.activation(mask_bytes[:, u % BYTE_SLOTS, :, :], adj_in[:, u % ADJ_SLOTS, :, :],
                                         ACT.Sigmoid, bias=sig_bias[:], scale=200.0).then_inc(bytes_ready, 1)
                    if first and 2 <= u < 2 + STRIPES - 1:
                        scale_xj(u - 1)

            def carry_wait(i):
                nc.scalar.copy(carried[:, i:i + 1], eps[:])

            def sum_rows(ib):
                act.wait_ge(y_ready, ib * T + T)
                carry_wait(0)
                for t in range(T):
                    last = nc.scalar.activation(unused[:, t, :], tile(ib * T + t), ACT.Identity, accum_out=total[:, t:t + 1])
                last.then_inc(total_ready, 1)

            def sum_squares(ib):
                act.wait_ge(mean_ready, ib + 1)
                carry_wait(1)
                for t in range(T):
                    last = nc.scalar.activation(unused[:, t, :], tile(ib * T + t), ACT.Square, bias=neg_mean[:, t:t + 1],
                                                accum_out=square_sum[:, t:t + 1])
                last.then_inc(squares_ready, 1)

            def normalise(ib):
                act.wait_ge(offset_ready, ib + 1)
                carry_wait(2)
                for t in range(T):
                    last = nc.scalar.activation(tile(ib * T + t), tile(ib * T + t), ACT.Identity, bias=offset[:, t:t + 1],
                                                scale=rstd[:, t:t + 1])
                last.then_inc(out_ready, 1)
                act.wait_ge(out_ready, ib + 1)
                act.dma_start(out_v[:, bass.ds(ib * T, T), :], xi[:, bass.ds(ib * T, T), :]).then_inc(stored, 16)

            to_bytes(0, 0, first=True)
            to_bytes(0, 1, first=True)
            to_bytes(0, 2, first=True)
            to_bytes(0, 3)
            act.wait_ge(s_i_ready, RB)
            q_factors(ROWS, N)
            with act.Fori(1, BLOCKS) as ib:
                to_bytes(ib, 0)
                to_bytes(ib, 1)
                sum_rows(ib - 1)
                to_bytes(ib, 2)
                sum_squares(ib - 1)
                to_bytes(ib, 3)
                normalise(ib - 1)
            act.wait_ge(consts_ready, 1)
            nc.scalar.activation(deviations[:, 0:1], eps[:], ACT.Sqrt).then_inc(last_deviation_ready, 1)
            act.wait_ge(last_deviation_ready, 1)

            def last_normalise(g):
                v = LAST_GROUPS[g]
                act.wait_ge(offset_ready, BLOCKS + g)
                for t in range(v.start, v.stop):
                    last = nc.scalar.activation(tile((BLOCKS - 1) * T + t), tile((BLOCKS - 1) * T + t), ACT.Identity,
                                                bias=offset[:, t:t + 1], scale=rstd[:, t:t + 1])
                last.then_inc(early_out_ready, 1)

            def last_deviations(g):
                v = LAST_GROUPS[g]
                act.wait_ge(moments_ready, v.stop)
                nc.scalar.activation(deviations[:, v], moments[:, v, 1], ACT.Sqrt, bias=eps[:]).then_inc(last_deviation_ready, 1)

            for g in range(EARLY - 1):
                last_normalise(g)
            last_deviations(EARLY)
            last_normalise(EARLY - 1)
            last_deviations(EARLY + 1)
            act.wait_ge(stored, 16 * (BLOCKS - 1))

            act.wait_ge(again_ready, 1)
            with act.If(act.value_load(again[0:1, 0:1], min_val=0, max_val=1) > 0):
                for m in range(TILES // 4):
                    act.wait_ge(x_turned, m + 1)
                    nc.scalar.copy(turned[:, m * BANK:(m + 1) * BANK], banks[m % 4][:, :]).then_inc(x_turned_ready, 1)
                for rb in range(RB):
                    act.wait_ge(s_j_in_psum, rb + 1)
                    nc.scalar.copy(s_j_row[:, rb * BANK:(rb + 1) * BANK], banks[rb][:, :]).then_inc(s_j_row_ready, 1)
                with act.Fori(0, TILES) as t:
                    act.wait_ge(scores_ready, t + 1)
                    nc.scalar.activation(scores, scores, ACT.Exp, bias=neg_max[:, 1:2],
                                         accum_out=den[:, 0:1]).then_inc(probs_ready, 1)
                    for m in range(CHUNKS // 4):
                        act.wait_ge(probs_turned, t * (CHUNKS // 4) + (m + 1))
                        nc.scalar.copy(turned[:, m * BANK:(m + 1) * BANK], banks[m % 4][:, :]).then_inc(turned_ready, 1)
                    act.wait_ge(mean_again, t + 1)
                    nc.scalar.activation(unused[:, 0, :], y[:, 0, :], ACT.Square, bias=neg_mean[:, 0:1],
                                         accum_out=square_sum[:, 0:1]).then_inc(squares_again, 1)
                    act.wait_ge(squares_again, t + 1)
                    nc.scalar.activation(deviation[:, 0:1], square_sum[:, 0:1], ACT.Sqrt, bias=eps[:],
                                         scale=1.0 / D).then_inc(deviation_ready, 1)
                    act.wait_ge(scale_ready, t + 1)
                    nc.scalar.activation(y[:, 1, :], y[:, 0, :], ACT.Identity, bias=offset[:, 0:1],
                                         scale=deviation[:, 1:2]).then_inc(row_out_ready, 1)
                    act.wait_ge(row_out_ready, t + 1)
                    act.dma_start(out[bass.ds(t * P, P), :], y[:, 1, :]).then_inc(row_stored, 16)
                    act.wait_ge(row_stored, 16 * t + 16)

        @block.vector
        def _(dve):
            def sum_products(st):
                c = slice(st * SC, (st + 1) * SC)
                dve.wait_ge(products_ready, st + 1)
                nc.vector.reduce_sum(s_j[:, c], prod[:, c, :], X).then_inc(s_j_ready, 1)

            dve.wait_ge(attn_j_loaded, 16)
            for st in range(STRIPES):
                dve.wait_ge(x_loaded[st], 16 * Q)
                c = slice(st * SC, (st + 1) * SC)
                nc.vector.tensor_tensor(prod[:, c, :], x_raw[:, c, :], attn_j[:].unsqueeze(1).broadcast_to([P, SC, D]),
                                        ALU.mult).then_inc(products_ready, 1)
                if st == 0:
                    dve.wait_ge(attn_loaded, 16)
                    dve.wait_ge(consts_ready, 1)
                    nc.vector.tensor_scalar(attn_iw[:], ones[:], attn_i[:], None, ALU.mult).then_inc(attn_wide, 1)
                elif st - 1 != S_J_BY_ACT:
                    sum_products(st - 1)
            sum_products(STRIPES - 1)

            def first_bytes(half):
                g = slice(half * G // 2, (half + 1) * G // 2)
                dve.wait_ge(adj_loaded[0] if half else first_half_loaded, 16 * Q)
                nc.vector.tensor_scalar(mask_bytes[:, 0, g, :], adj_in[:, 0, g, :], 0.0, None,
                                        ALU.is_gt).then_inc(first_bytes_ready, 1)

            dve.wait_ge(s_j_ready, STRIPES - 1)
            dve.wait_ge(s_j_by_act_ready, 1)
            nc.vector.reduce_max(smax[:, 0:1], s_j[:], X).then_inc(row_max_ready, 1)
            dve.wait_ge(max_turned, 1)
            nc.vector.reduce_max(smax[0:1, 1:2], banks[S_BANK][0:1, 0:P], X).then_inc(max_found, 1)
            first_bytes(0)
            dve.wait_ge(max_spread, 1)
            nc.vector.tensor_scalar(shift[:, 0:1], banks[S_BANK][:, P:P + 1], SLOPE - 1, None, ALU.mult)
            nc.vector.tensor_scalar(shift[:, 1:2], banks[S_BANK][:, P:P + 1], -SLOPE, None, ALU.mult)
            nc.vector.tensor_copy(shift[:, 2:3], banks[S_BANK][:, P:P + 1]).then_inc(shift_ready, 1)

            def turn(st, h, groups):
                src = mask_bytes[:, (st * H + h) % BYTE_SLOTS, :, :].bitcast(u32).rearrange("p g (f w) -> p g f w", w=B)
                dst = mask_t[:, st % 2, :, :, :].rearrange("p f i k -> p f (i k)").bitcast(u32)
                dst = dst[:, :, h * UROWS:(h + 1) * UROWS].rearrange("p f (g a) -> p g f a", a=B)
                return nc.vector.transpose(dst[:, groups, :, :], src[:, groups, :, :])

            def turn_unit(ib, st, h):
                dve.wait_ge(bytes_ready, ib * UNITS + (st * H + h))
                turn(st, h, slice(0, G)).then_inc(mask_ready, 1)

            dve.wait_ge(first_bytes_ready, 1)
            turn(0, 0, slice(0, G // 2))
            dve.wait_ge(factors_ready, 1)
            nc.vector.tensor_tensor(xj[:, 0:SC, 0:D], x_raw[:, 0:SC, :], d_j[:, 0:SC].unsqueeze(2).broadcast_to([P, SC, D]),
                                    ALU.mult).then_inc(first_xj_scaled, 1)
            first_bytes(1)
            dve.wait_ge(first_bytes_ready, 2)
            turn(0, 0, slice(G // 2, G)).then_inc(mask_ready, 1)

            def residual(ib, part, final=False):

                def largest_inverse():
                    dve.wait_ge(rden_ready, calls + len(groups))
                    dve.wait_ge(worst_ready, ib + 1)
                    nc.vector.tensor_tensor(worst[:, 0:T], worst[:, 0:T], rden[:], ALU.max).then_inc(worst_ready, 1)
                    if final:
                        dve.wait_ge(worst_ready, ib + 2)
                        nc.vector.reduce_max(worst[:, T:T + 1], worst[:, 0:T], X).then_inc(worst_found, 1)

                groups = LAST_GROUPS if final else GROUPS
                calls = ib * len(GROUPS)

                def denominators(g):
                    v = groups[g]
                    if v.stop < T:
                        dve.wait_ge(tile_summed, ib * (T - 1) + v.stop)
                    else:
                        dve.wait_ge(weights_used, ib * CHUNKS + CHUNKS)
                    nc.vector.tensor_scalar(rden[:, v], psum[:, v, D], LEAST, None, ALU.max).then_inc(den_ready, 1)

                def invert(g):
                    v = groups[g]
                    dve.wait_ge(den_ready, calls + (g + 1))
                    nc.vector.reciprocal(rden[:, v], rden[:, v]).then_inc(rden_ready, 1)

                def add_x(g):
                    dve.wait_ge(rden_ready, calls + (g + 1))
                    for t in range(groups[g].start, groups[g].stop):
                        nc.vector.scalar_tensor_tensor(tile(ib * T + t), banks[t][:, 0:D], rden[:, t:t + 1], tile(ib * T + t),
                                                       ALU.mult, ALU.add).then_inc(y_ready, 1)

                def mean_and_variance(g):
                    tiles = range(groups[g].start, groups[g].stop)
                    for t in tiles:
                        dve.wait_ge(y_ready, ib * T + (t + 1))
                        nc.vector.bn_stats(half_moments[:, t, :], tile(ib * T + t)).then_inc(half_moments_ready, 1)
                    for t in tiles:
                        dve.wait_ge(half_moments_ready, t + 1)
                        nc.vector.bn_aggr(moments[:, t, :], half_moments[:, t, :]).then_inc(moments_ready, 1)

                def normalise(g):
                    v = groups[g]
                    dve.wait_ge(last_deviation_ready, g - EARLY + 2)
                    nc.vector.reciprocal(rstd[:, v], deviations[:, v]).then_inc(last_rstd_ready, 1)
                    dve.wait_ge(last_rstd_ready, g - EARLY + 1)
                    for t in range(v.start, v.stop):
                        last = nc.vector.tensor_scalar(tile(ib * T + t), tile(ib * T + t), moments[:, t, 0:1], rstd[:, t:t + 1],
                                                       ALU.subtract, ALU.mult)
                    last.then_inc(last_out_ready, 1)

                if final:
                    for g in range(len(groups) + 1):
                        if g < len(groups):
                            denominators(g)
                            invert(g)
                            add_x(g)
                            mean_and_variance(g)
                        if g == len(groups):
                            largest_inverse()
                        if g > EARLY:
                            normalise(g - 1)
                else:
                    denominators(part)
                    invert(part)
                    add_x(part)
                    if part == len(groups) - 1:
                        largest_inverse()

            def weigh(ib, c, rows, first=False):
                if not first or c >= W_SLOTS:
                    dve.wait_ge(weights_used, ib * CHUNKS + (c - W_SLOTS + 1))
                nc.vector.scalar_tensor_tensor(
                    weights[:, c % W_SLOTS, rows], q_row[:, bass.ds(ib * ROWS + rows.start, rows.stop - rows.start)],
                    r_j[:, c:c + 1], mask_t[:, c // SC % 2, c % SC // K, rows, c % K],
                    ALU.max, ALU.mult).then_inc(weights_ready, 1)

            def stripe(ib, st, final=False):
                dve.wait_ge(mask_ready, ib * UNITS + (st + 1) * H)
                for s in range(SC):
                    c = st * SC + s
                    weigh(ib, c, slice(0, ROWS))
                    if s in TURN_AT and not (final and st == STRIPES - 1):
                        dve.wait_ge(weights_ready, ib * CHUNKS + (CHUNKS + st * SC))
                        if st + 1 < STRIPES:
                            turn_unit(ib, st + 1, TURN_AT.index(s))
                        else:
                            turn_unit(ib + 1, 0, TURN_AT.index(s))
                    if c == RESIDUAL_AT:
                        residual(ib - 1, 1)
                if st == STRIPES - 1 and not final:
                    dve.wait_ge(xi_loaded, 16)
                    residual(ib, 0)

            for st in range(STRIPES):
                for h in range(H):
                    if st == 0:
                        if h == 1:
                            turn_unit(0, 0, h)
                        dve.wait_ge(q_ready, h + 1)
                    dve.wait_ge(mask_ready, st * H + h + 1)
                    for s in range(SC):
                        if st == 0 and h == 0 and s == xT_slot:
                            dve.wait_ge(s_i_in_psum, RB)
                        weigh(0, st * SC + s, slice(h * UROWS, (h + 1) * UROWS), first=True)
                        if (st, h, s) in FIRST_TURNS:
                            st1, h1 = FIRST_TURNS[st, h, s]
                            if st1 >= 2:
                                dve.wait_ge(weights_ready, 2 * (st1 - 1) * SC)
                            turn_unit(0, st1, h1)
            dve.wait_ge(weights_ready, 2 * (STRIPES - 1) * SC)
            turn_unit(1, 0, 0)
            dve.wait_ge(first_xi_loaded, 16)
            residual(0, 0)
            turn_unit(1, 0, 1)
            dve.wait_ge(q_ready, H + 1)
            with dve.Fori(1, BLOCKS - 1) as ib:
                for st in range(STRIPES):
                    stripe(ib, st)
            for st in range(STRIPES):
                stripe(BLOCKS - 1, st, final=True)
            residual(BLOCKS - 1, 0, final=True)

            dve.wait_ge(worst_turned, 1)
            nc.vector.reduce_max(worst[0:1, T + 1:T + 2], banks[0][0:1, 0:P], X).then_inc(worst_found, 1)
            dve.wait_ge(worst_found, 2)
            nc.vector.tensor_scalar(again[:], worst[0:1, T + 1:T + 2], MOST, None, ALU.is_gt).then_inc(again_ready, 1)

            dve.wait_ge(again_ready, 1)
            with dve.If(dve.value_load(again[0:1, 0:1], min_val=0, max_val=1) > 0):
                dve.wait_ge(inputs_again, 48)
                nc.vector.tensor_scalar(attn_iw[:], ones[:], attn_col[:], None, ALU.mult).then_inc(wide_again, 1)
                nc.vector.tensor_tensor(leaky.rearrange("p (t d) -> p t d", t=TILES), xi[:],
                                        attn_row[:].unsqueeze(1).broadcast_to([P, TILES, D]),
                                        ALU.mult).then_inc(s_i_products, 1)
                dve.wait_ge(s_i_products, 1)
                nc.vector.reduce_sum(s_i[:], leaky.rearrange("p (t d) -> p t d", t=TILES), X).then_inc(adj_rows_free, 1)
                dve.wait_ge(adj_rows_free, 1)
                dve.wait_ge(s_j_row_ready, RB)
                with dve.Fori(0, TILES) as t:
                    nc.vector.tensor_scalar(scores, s_j_row[:], s_i[:, bass.ds(t, 1)], None, ALU.add).then_inc(score_step, 1)
                    dve.wait_ge(score_step, t * 4 + 1)
                    nc.vector.scalar_tensor_tensor(leaky, scores, SLOPE, scores, ALU.mult, ALU.max).then_inc(score_step, 1)
                    dve.wait_ge(score_step, t * 4 + 2)
                    dve.wait_ge(adj_rows_loaded, 16 * t + 16)
                    nc.vector.tensor_scalar(scores, adj_rows, 0.0, NEG_INF, ALU.is_le, ALU.mult).then_inc(adj_rows_free, 1)
                    dve.wait_ge(adj_rows_free, t + 2)
                    nc.vector.tensor_tensor(scores, scores, leaky, ALU.add).then_inc(score_step, 1)
                    dve.wait_ge(score_step, t * 4 + 3)
                    nc.vector.reduce_max(neg_max[:, 0:1], scores, X).then_inc(score_step, 1)
                    dve.wait_ge(score_step, t * 4 + 4)
                    nc.vector.tensor_scalar(neg_max[:, 1:2], neg_max[:, 0:1], -1.0, None, ALU.mult).then_inc(scores_ready, 1)
                    dve.wait_ge(sum_ready, t + 1)
                    nc.vector.reciprocal(den[:, 1:2], den[:, 0:1]).then_inc(row_step, 1)
                    dve.wait_ge(row_step, t * 4 + 1)
                    nc.vector.scalar_tensor_tensor(y[:, 0, :], banks[4][:, 0:D], den[:, 1:2],
                                                   xi[:, bass.ds(t, 1), :].rearrange("p o d -> p (o d)"),
                                                   ALU.mult, ALU.add).then_inc(row_step, 1)
                    dve.wait_ge(row_step, t * 4 + 2)
                    nc.vector.reduce_sum(total[:, 0:1], y[:, 0, :], X).then_inc(row_step, 1)
                    dve.wait_ge(row_step, t * 4 + 3)
                    nc.vector.tensor_scalar(neg_mean[:, 0:1], total[:, 0:1], -1.0 / D, None, ALU.mult).then_inc(mean_again, 1)
                    dve.wait_ge(deviation_ready, t + 1)
                    nc.vector.reciprocal(deviation[:, 1:2], deviation[:, 0:1]).then_inc(row_step, 1)
                    dve.wait_ge(row_step, t * 4 + 4)
                    nc.vector.tensor_tensor(offset[:, 0:1], neg_mean[:, 0:1], deviation[:, 1:2],
                                            ALU.mult).then_inc(scale_ready, 1)
                    dve.wait_ge(row_stored, 16 * t + 16)

        @block.tensor
        def _(pe):
            pe.wait_ge(consts_ready, 1)
            for _ in range(WARM):
                nc.tensor.transpose(banks[S_BANK][:, 0:P], ident[:], ident[:])

            def turn_x(m):
                if m % F == 0:
                    pe.wait_ge(x_loaded[m // F], 16 * Q)
                if m >= 4:
                    pe.wait_ge(xT_ready, m - 3)
                for k in range(K):
                    last = nc.tensor.transpose(banks[XT_BANK + m % 4][:, k * P:(k + 1) * P], x_raw[:, m * K + k, :], ident[:])
                last.then_inc(xT_in_psum, 1)

            def s_i_piece(rb):
                pe.wait_ge(attn_wide, 1)
                bank = S_I_BANK[rb]
                pe.wait_ge(xT_ready, max(rb + 1, bank - XT_BANK + 5 if bank >= XT_BANK else 0))
                nc.tensor.matmul(banks[bank][:, :], attn_iw[:], xT[:, rb * BANK:(rb + 1) * BANK],
                                 start=True, stop=True).then_inc(s_i_in_psum, 1)

            for m in range(CHUNKS // K):
                turn_x(m)
                if m in (2, 4, 5):
                    s_i_piece((2, 4, 5).index(m))
            s_i_piece(3)
            pe.wait_ge(row_max_ready, 1)
            nc.tensor.transpose(banks[S_BANK][0:1, 0:P], smax[:, 0:1], ident[:]).then_inc(max_turned, 1)
            s_i_piece(4)
            pe.wait_ge(max_found, 1)
            nc.tensor.matmul(banks[S_BANK][:, P:P + 1], ones[0:1, :], smax[0:1, 1:2], start=True, stop=True).then_inc(max_spread, 1)
            s_i_piece(5)
            s_i_piece(6)
            pe.wait_ge(shift_ready, 1)
            s_i_piece(7)

            pe.wait_ge(s_i_ready, 1)
            for _ in range(KEEP_WARM):
                nc.tensor.transpose(banks[S_I_BANK[0]][:, 0:P], ident[:], ident[:])

            def product(c, t):
                return nc.tensor.matmul(banks[t][:, 0:D1], weights[:, c % W_SLOTS, t * P:(t + 1) * P],
                                        xj[:, c, 0:D1], start=(c == 0), stop=(c == CHUNKS - 1))

            def last_products(tiles, weights_before):
                for t in tiles:
                    for c in range(CHUNKS - LAST, CHUNKS):
                        if t == tiles[0]:
                            pe.wait_ge(weights_ready, weights_before + (c + 1))
                        last = product(c, t)
                        if t == T - 1:
                            last.then_inc(weights_used, 1)
                    if t < T - 1:
                        last.then_inc(tile_summed, 1)

            for st in range(STRIPES):
                if st == 0:
                    pe.wait_ge(first_xj_scaled, 1)
                else:
                    pe.wait_ge(xj_scaled, st)
                for h in range(H):
                    tiles = range(h * T // H, (h + 1) * T // H)
                    if st == 0:
                        pe.wait_ge(s_i_ready, RB if h else T // H)
                    for c in range(st * SC, min((st + 1) * SC, CHUNKS - LAST)):
                        pe.wait_ge(weights_ready, (st + h) * SC + (c + 1))
                        for t in tiles:
                            last = product(c, t)
                        if h == H - 1:
                            last.then_inc(weights_used, 1)
                    if st == STRIPES - 1:
                        last_products(tiles, (st + h) * SC)

            def row_block(ib):
                for c in range(CHUNKS - LAST):
                    pe.wait_ge(weights_ready, ib * CHUNKS + (CHUNKS + c + 1))
                    for t in range(T):
                        if c == 0:
                            pe.wait_ge(y_ready, (ib - 1) * T + (t + 1))
                        last = product(c, t)
                    last.then_inc(weights_used, 1)
                last_products(range(T), ib * CHUNKS + CHUNKS)

            with pe.Fori(1, BLOCKS) as ib:
                row_block(ib)

            pe.wait_ge(worst_found, 1)
            nc.tensor.transpose(banks[0][0:1, 0:P], worst[:, T:T + 1], ident[:]).then_inc(worst_turned, 1)

            pe.wait_ge(again_ready, 1)
            with pe.If(pe.value_load(again[0:1, 0:1], min_val=0, max_val=1) > 0):
                pe.wait_ge(inputs_again, 48)
                for m in range(TILES // 4):
                    if m >= 4:
                        pe.wait_ge(x_turned_ready, m - 3)
                    for k in range(4):
                        last = nc.tensor.transpose(banks[m % 4][:, k * P:(k + 1) * P], xi[:, m * 4 + k, :], ident[:])
                    last.then_inc(x_turned, 1)
                pe.wait_ge(x_turned_ready, TILES // 4)
                pe.wait_ge(wide_again, 1)
                for rb in range(RB):
                    nc.tensor.matmul(banks[rb][:, :], attn_iw[:], turned[:, rb * BANK:(rb + 1) * BANK],
                                     start=True, stop=True).then_inc(s_j_in_psum, 1)
                pe.wait_ge(s_j_row_ready, RB)
                with pe.Fori(0, TILES) as t:
                    pe.wait_ge(probs_ready, t + 1)
                    for m in range(CHUNKS // 4):
                        if m >= 4:
                            pe.wait_ge(turned_ready, t * (CHUNKS // 4) + (m - 3))
                        for k in range(4):
                            c = m * 4 + k
                            last = nc.tensor.transpose(banks[m % 4][:, k * P:(k + 1) * P],
                                                       scores[:, c * P:(c + 1) * P], ident[:])
                        last.then_inc(probs_turned, 1)
                    pe.wait_ge(turned_ready, t * (CHUNKS // 4) + CHUNKS // 4)
                    for c in range(CHUNKS):
                        last = nc.tensor.matmul(banks[4][:, 0:D], turned[:, c * P:(c + 1) * P], xi[:, c, :],
                                                start=(c == 0), stop=(c == CHUNKS - 1))
                    last.then_inc(sum_ready, 1)


_INS = ['x', 'adj', 'L0_gnn_attn']


def kernel(**inputs):
    import numpy as _np
    import concourse.bacc as _bacc
    from concourse import mybir as _mybir
    from concourse.bass_utils import run_bass_kernel_spmd as _run

    nc = _bacc.Bacc("TRN2", target_bir_lowering=False, num_devices=1)
    arrays, args = {}, []
    for name in _INS:
        a = _np.ascontiguousarray(inputs[name])
        arrays[f"in_{name}_dram"] = a
        args.append(nc.dram_tensor(f"in_{name}_dram", a.shape, _mybir.dt.from_np(a.dtype), kind="ExternalInput").ap())
    args.append(nc.dram_tensor("out_0_dram", (4096, 128), _mybir.dt.float32, kind="ExternalOutput").ap())
    gat_kernel(nc, *args)
    r = _run(nc, [arrays], core_ids=[0])
    return r.results[0]["out_0_dram"]
```
